# Optimizing a Trainium2 kernel written in Bass

```python
import numpy as np
import jax
import jax.numpy as jnp

def _softmax(x, axis=-1):
    return jax.nn.softmax(x, axis=axis)

def _gelu(x):
    return jax.nn.gelu(x, approximate=True)

def _silu(x):
    return jax.nn.silu(x)

def _sigmoid(x):
    return jax.nn.sigmoid(x)

def _layernorm(x, axis=-1, eps=1e-05):
    m = jnp.mean(x, axis=axis, keepdims=True)
    v = jnp.var(x, axis=axis, keepdims=True)
    return (x - m) / jnp.sqrt(v + eps)

def _scatter_add(tgt, idx, src, axis=0):
    return tgt.at[idx].add(src)

def _segment_sum(src, seg, n):
    return jax.ops.segment_sum(src, seg, n)
kernel_name = 'mk_rec_standalone_d1_rec_r8_13c186'

def setup_inputs(seed: int=0):
    np.random.seed(seed)
    _w = jnp.asarray

    def _rec_inputs():
        import jax
        import jax.numpy as jnp
        _rk = jax.random.key(seed)
        r_x = jax.random.randint(jax.random.fold_in(_rk, 1), (512, 26, 8), 0, 125000, jnp.int32)
        return r_x
    r_x = _rec_inputs()

    def _L0_rec_setup():
        import jax, jax.numpy as jnp
        import numpy as np
        V = 125000
        D = 64
        F = 26
        L = 8
        B = 512
        IN_DIM = F * D
        HIDDENS = (1024, 1024, 512)
        key = jax.random.key(seed)
        ks = jax.random.split(key, 4 + 4 * len(HIDDENS))
        inp = {}
        inp['x'] = jax.random.randint(ks[0], (B, F, L), 0, V, dtype=jnp.int64)
        inp['emb_table'] = jax.random.normal(ks[1], (V, D), dtype=jnp.float32) * 0.01
        ki = 2
        for i, h in enumerate(HIDDENS):
            inp[f'w1_{i}'] = jax.random.normal(ks[ki], (IN_DIM, h), dtype=jnp.float32) * 0.02
            inp[f'b1_{i}'] = jnp.zeros((h,), dtype=jnp.float32)
            inp[f'w2_{i}'] = jax.random.normal(ks[ki + 1], (h, IN_DIM), dtype=jnp.float32) * 0.02
            inp[f'b2_{i}'] = jnp.zeros((IN_DIM,), dtype=jnp.float32)
            ki += 2
        inp['lin_w'] = jax.random.normal(ks[ki], (IN_DIM, 1), dtype=jnp.float32) * 0.02
        inp['lin_b'] = jnp.zeros((1,), dtype=jnp.float32)
        return inp
    _L0_rec_all = _L0_rec_setup()
    _L0_rec_in = {k: v for k, v in _L0_rec_all.items() if k in ('emb_table', 'w1_0', 'b1_0', 'w2_0', 'b2_0', 'w1_1', 'b1_1', 'w2_1', 'b2_1', 'w1_2', 'b1_2', 'w2_2', 'b2_2', 'lin_w', 'lin_b')}
    del _L0_rec_all
    return {'r_x': r_x, 'L0_rec_emb_table': _L0_rec_in['emb_table'], 'L0_rec_w1_0': _L0_rec_in['w1_0'], 'L0_rec_b1_0': _L0_rec_in['b1_0'], 'L0_rec_w2_0': _L0_rec_in['w2_0'], 'L0_rec_b2_0': _L0_rec_in['b2_0'], 'L0_rec_w1_1': _L0_rec_in['w1_1'], 'L0_rec_b1_1': _L0_rec_in['b1_1'], 'L0_rec_w2_1': _L0_rec_in['w2_1'], 'L0_rec_b2_1': _L0_rec_in['b2_1'], 'L0_rec_w1_2': _L0_rec_in['w1_2'], 'L0_rec_b1_2': _L0_rec_in['b1_2'], 'L0_rec_w2_2': _L0_rec_in['w2_2'], 'L0_rec_b2_2': _L0_rec_in['b2_2'], 'L0_rec_lin_w': _L0_rec_in['lin_w'], 'L0_rec_lin_b': _L0_rec_in['lin_b']}

def reference(r_x, L0_rec_emb_table, L0_rec_w1_0, L0_rec_b1_0, L0_rec_w2_0, L0_rec_b2_0, L0_rec_w1_1, L0_rec_b1_1, L0_rec_w2_1, L0_rec_b2_1, L0_rec_w1_2, L0_rec_b1_2, L0_rec_w2_2, L0_rec_b2_2, L0_rec_lin_w, L0_rec_lin_b):
    import jax
    import jax.numpy as jnp

    def _L0_rec_ref(x, emb_table, w1_0, b1_0, w2_0, b2_0, w1_1, b1_1, w2_1, b2_1, w1_2, b1_2, w2_2, b2_2, lin_w, lin_b):
        import jax, jax.numpy as jnp
        import numpy as np
        V = 125000
        D = 64
        F = 26
        L = 8
        B = 512
        IN_DIM = F * D
        HIDDENS = (1024, 1024, 512)
        pooled = emb_table[x].sum(axis=2)
        feat = pooled.reshape(x.shape[0], -1)
        for w1, b1, w2, b2 in ((w1_0, b1_0, w2_0, b2_0), (w1_1, b1_1, w2_1, b2_1), (w1_2, b1_2, w2_2, b2_2)):
            h = jax.nn.relu(feat @ w1 + b1)
            feat = jax.nn.relu(h @ w2 + b2 + feat)
        return jax.nn.sigmoid(feat @ lin_w + lin_b)
    y = _L0_rec_ref(r_x, L0_rec_emb_table, L0_rec_w1_0, L0_rec_b1_0, L0_rec_w2_0, L0_rec_b2_0, L0_rec_w1_1, L0_rec_b1_1, L0_rec_w2_1, L0_rec_b2_1, L0_rec_w1_2, L0_rec_b1_2, L0_rec_w2_2, L0_rec_b2_2, L0_rec_lin_w, L0_rec_lin_b)
    return y

_drawn_inputs = setup_inputs


def setup_inputs(seed=0):
    import zlib

    import numpy as np

    out = dict(_drawn_inputs(seed))
    spreads = {'L0_rec_b1_0': (0.0, 0.8),
     'L0_rec_b2_0': (0.0, 0.429),
     'L0_rec_b1_1': (0.0, 0.8),
     'L0_rec_b2_1': (0.0, 0.8),
     'L0_rec_b1_2': (0.0, 2.0),
     'L0_rec_b2_2': (0.0, 2.0)}
    factors = {'L0_rec_emb_table': 8.0,
     'L0_rec_w1_0': 8.0,
     'L0_rec_w2_0': 8.0,
     'L0_rec_w1_1': 8.0,
     'L0_rec_w1_2': 6.874,
     'L0_rec_w2_2': 3.453}
    for name, (base, spread) in spreads.items():
        noise = np.random.default_rng([zlib.crc32(name.encode()), seed]).standard_normal(out[name].shape)
        drawn = base * np.exp(spread * noise) if base else spread * noise
        out[name] = jnp.asarray(drawn.astype(out[name].dtype))
    for name, factor in factors.items():
        out[name] = (out[name] * factor).astype(out[name].dtype)
    return out
```

```python
from contextlib import ExitStack

import concourse.bass as bass
from concourse import mybir

F32 = mybir.dt.float32
I32 = mybir.dt.int32
ALU = mybir.AluOpType
ACT = mybir.ActivationFunctionType

P = 128
BATCH, FIELDS, LOOKUPS, DIM = 512, 26, 8, 64
IN_DIM = FIELDS * DIM
HIDDENS = (1024, 1024, 512)
FC = IN_DIM // P
HC = [h // P for h in HIDDENS]

GB = 32
QUARTERS = P // GB
HALVES = LOOKUPS // QUARTERS
GROUPS = BATCH // GB
GATHERS = HALVES * FIELDS

QUADS = 4
QCHUNKS = FC // QUADS
REST = P // QUADS
QUAD = QCHUNKS * P + REST

LOOP_TILES = 2
TILES = [128, 128, 128, 64, 64]
POOLED_AFTER = [[1, 1, 2], [1, 1, 2], [1, 1, 0], [1, 0, 1], [0, 0, 0]]

STREAMED = (("w1", 0), ("w2", 0), ("w1", 1))
SLABS = FC + HC[0] + FC
SLOTS = 6

IDENT, SEL, CONSTS = 0, P, P + GB
B1 = [0, HC[0], HC[0] + HC[1]]
B2 = [sum(HC) + FC * n for n in range(3)]
LIN_W = sum(HC) + 3 * FC
PARAMS = LIN_W + FC


class Tile:

    def __init__(self, m):
        self.m = m
        self.side = P // m
        self.f_blocks = QUADS // self.side
        self.f_units = self.f_blocks + 1

    def h_width(self, n):
        return min(512, HIDDENS[n] // self.side)

    def h_blocks(self, n):
        return HIDDENS[n] // self.side // self.h_width(n)

    def h_order(self, n):
        per, blocks = self.h_width(n) // P, self.h_blocks(n)
        return [((j * blocks + s) * per + i, s) for s in range(blocks) for j in range(self.side) for i in range(per)]

    def f_order(self):
        out = [(QCHUNKS * (j * self.f_blocks + s) + i, s)
               for s in range(self.f_blocks) for j in range(self.side) for i in range(QCHUNKS)]
        return out + [(FC - 1, self.f_blocks)]

    def units_before(self, n, features):
        return sum(self.h_blocks(i) + self.f_units for i in range(n)) + (self.h_blocks(n) if features else 0)

    def banks_before(self, n, features):
        return sum(self.h_blocks(i) + self.f_blocks for i in range(n)) + (self.h_blocks(n) if features else 0)

    def slabs(self):
        return ([(("w1", 0), k) for k in range(FC)] + [(("w2", 0), k) for k, _ in self.h_order(0)]
                + [(("w1", 1), k) for k, _ in self.f_order()])


def slot_loads(slot):
    return len(range(slot, SLABS, SLOTS))


class Base:

    def __init__(self, index, tile):
        full = Tile(TILES[0])
        self.tile = tile
        self.units = self.banks = self.batches = self.groups = 0
        self.index = index
        if isinstance(index, int) and index >= LOOP_TILES:
            before = [Tile(m) for m in TILES[:index]]
            self.units = sum(x.units_before(3, False) for x in before)
            self.banks = sum(x.banks_before(3, False) for x in before)
            self.batches = sum(x.m for x in before)
            self.groups = TILES[0] // GB + sum(sum(p) for p in POOLED_AFTER[:index])
        else:
            self.units = index * full.units_before(3, False)
            self.banks = index * full.banks_before(3, False)
            self.batches = index * full.m
            self.groups = index * sum(POOLED_AFTER[0]) + TILES[0] // GB


def over_tiles(eng, body):
    with eng.Fori(0, LOOP_TILES) as t:
        body(Base(t, Tile(TILES[0])), POOLED_AFTER[0], False)
    for t in range(LOOP_TILES, len(TILES)):
        body(Base(t, Tile(TILES[t])), POOLED_AFTER[t], t == len(TILES) - 1)


def units3(ap, tile, per, blocks, s):
    return ap.rearrange("p (j s i) b -> p s i j b", j=tile.side, s=blocks, i=per)[:, s]


def recommender(nc, idx_d, table_d, consts_d, params_d, lin_b_d, w1_d, w2_d, out_d):
    with ExitStack() as ctx:
        def sb(name, shape, dt=F32):
            return ctx.enter_context(nc.sbuf_tensor(name, shape, dt))

        def sem(name):
            return ctx.enter_context(nc.semaphore(name))

        idx_all = sb("idx_all", [P, GROUPS * GATHERS], I32)
        idx_now = [sb(f"idx_now{i}", [P, GATHERS], I32) for i in range(2)]
        rows = [sb(f"rows{i}", [P, HALVES, IN_DIM]) for i in range(2)]
        pooled = sb("pooled", [P, FC, P])
        feat = sb("feat", [P, FC, P])
        hidden = sb("hidden", [P, max(HC), P])
        by_batch = sb("by_batch", [P, QUADS * QUAD])
        summed = [sb(f"summed{i}", [P, 512]) for i in range(2)]
        consts = sb("consts", [P, CONSTS])
        params = sb("params", [P, PARAMS])
        lin_b = sb("lin_b", [1, 1])
        y = sb("y", [1, BATCH])
        slots = [sb(f"slot{i}", [P, IN_DIM]) for i in range(SLOTS)]
        kept = {("w2", 1): sb("kept_w2_1", [P, HC[1], IN_DIM]),
                ("w1", 2): sb("kept_w1_2", [P, FC, HIDDENS[2]]),
                ("w2", 2): sb("kept_w2_2", [P, HC[2], IN_DIM])}
        ident = consts[:, IDENT:IDENT + P]
        sel = consts[:, SEL:SEL + GB]

        def bank(name):
            return ctx.enter_context(nc.psum_tensor(name, [P, 512], F32))

        acc = [bank(f"acc{i}") for i in range(QUADS)]
        turned = [bank(f"turned{i}") for i in range(2)]
        pool_ps = bank("pool_ps")
        lin_ps = bank("lin_ps")

        idx_in = sem("idx_in")
        small_in = sem("small_in")
        kept_in = {("w2", 1): sem("kept_w2_1_in"), ("w1", 2): sem("kept_w1_2_in"), ("w2", 2): sem("kept_w2_2_in")}
        slot_in = [sem(f"slot_in{i}") for i in range(SLOTS)]
        slabs_used = sem("slabs_used")
        idx_copied = sem("idx_copied")
        gathered = [sem(f"gathered{i}") for i in range(2)]
        halves_added = sem("halves_added")
        group_turned = sem("group_turned")
        group_pooled = sem("group_pooled")
        bank_done = sem("bank_done")
        bank_copied = sem("bank_copied")
        unit_turned = sem("unit_turned")
        unit_added = sem("unit_added")
        unit_ready = sem("unit_ready")
        residual_ready = sem("residual_ready")
        lin_done = sem("lin_done")
        y_ready = sem("y_ready")
        stored = sem("stored")

        block = ctx.enter_context(nc.Block())

        @block.sync
        def _(sp):
            sp.dma_start(idx_all[:, :], idx_d).then_inc(idx_in, 16)
            sp.dma_start(consts[:, :], consts_d).then_inc(small_in, 16)
            sp.dma_start(params[:, :], params_d).then_inc(small_in, 16)
            sp.dma_start(lin_b[:, :], lin_b_d).then_inc(small_in, 16)

            def load(tile, i):
                (kind, n), k = tile.slabs()[i]
                source = (w1_d if kind == "w1" else w2_d)[n][k * P:(k + 1) * P, :]
                sp.dma_start(slots[i % SLOTS][:, 0:source.shape[1]], source).then_inc(slot_in[i % SLOTS], 16)

            for i in range(SLOTS):
                load(Tile(TILES[0]), i)

            def body(base, pooled_after, last):
                for i in range(SLOTS, SLABS):
                    sp.wait_ge(slabs_used, base.index * SLABS + i - SLOTS + 1)
                    load(base.tile, i)
                if not last:
                    for i in range(SLOTS):
                        sp.wait_ge(slabs_used, base.index * SLABS + max(range(i, SLABS, SLOTS)) + 1)
                        load(base.tile, i)

            over_tiles(sp, body)
            sp.wait_ge(y_ready, len(TILES))
            sp.dma_start(out_d, y[:, :]).then_inc(stored, 16)
            sp.wait_ge(stored, 16)

        @block.gpsimd
        def _(pool):
            half_way = GATHERS // 2

            def copy_indices(buf, group, part):
                nc.gpsimd.tensor_copy(idx_now[buf][:, part * half_way:(part + 1) * half_way],
                                      idx_all[:, bass.ds(group * GATHERS + part * half_way, half_way)],
                                      ).then_inc(idx_copied, 1)

            def gather(buf, group, first_two=False, last=False):
                pool.wait_ge(idx_copied, group * 2 + 1)
                if not first_two:
                    pool.wait_ge(group_turned, group - 1)
                copy_indices(buf, group, 1)
                for g in range(GATHERS):
                    if g == half_way:
                        if not isinstance(group, int) or group:
                            pool.wait_ge(gathered[1 - buf], (group + buf) * (8 * GATHERS))
                        pool.wait_ge(idx_copied, group * 2 + 2)
                        if not last:
                            copy_indices(1 - buf, group + 1, 0)
                    half, field = g % HALVES, g // HALVES
                    nc.gpsimd.indirect_dma_start(
                        rows[buf][:, half, field * DIM:(field + 1) * DIM], None, table_d,
                        bass.IndirectOffsetOnAxis(ap=idx_now[buf][:, g:g + 1], axis=0),
                    ).then_inc(gathered[buf], 16)

            pool.wait_ge(idx_in, 16)
            copy_indices(0, 0, 0)
            for group in range(3):
                gather(group % 2, group, first_two=group < 2)
            with pool.Fori(0, (GROUPS - 4) // 2) as pair:
                gather(1, pair * 2 + 3)
                gather(0, pair * 2 + 4)
            gather(1, GROUPS - 1, last=True)

        @block.vector
        def _(dve):
            def add_halves(group, buf):
                dve.wait_ge(gathered[buf], (group + 2 - buf) * (8 * GATHERS))
                nc.vector.tensor_tensor(rows[buf][:, 0, :], rows[buf][:, 0, :], rows[buf][:, 1, :],
                                        ALU.add).then_inc(halves_added, 1)

            def add(unit, u, out, turned_ap, other):
                dve.wait_ge(unit_turned, unit + 1)
                if u >= 2:
                    dve.wait_ge(unit_ready, unit - 1)
                nc.vector.tensor_tensor(out, turned_ap, other, ALU.add).then_inc(unit_added, 1)

            def body(base, pooled_after, last):
                tile, m = base.tile, base.tile.m
                group = 0
                for n in range(3):
                    blocks, per = tile.h_blocks(n), tile.h_width(n) // P
                    bias = params[:, B1[n]:B1[n] + HC[n]].unsqueeze(2).to_broadcast([P, HC[n], m])
                    for s in range(blocks):
                        u = tile.units_before(n, False) + s
                        shape = dict(i=per, j=tile.side)
                        add(base.units + u, u,
                            summed[u % 2][:, 0:per * P].rearrange("p (i j b) -> p i j b", **shape),
                            turned[u % 2][:, 0:per * P].rearrange("p (i j b) -> p i j b", **shape),
                            units3(bias, tile, per, blocks, s))
                    if n == 0:
                        dve.wait_ge(group_pooled, base.groups)
                    dve.wait_ge(bank_done, base.banks + tile.banks_before(n, True))
                    nc.vector.tensor_tensor(feat[:, :, 0:m], (feat if n else pooled)[:, :, 0:m],
                                            params[:, B2[n]:B2[n] + FC].unsqueeze(2).to_broadcast([P, FC, m]),
                                            ALU.add).then_inc(residual_ready, 1)
                    dve.wait_ge(residual_ready, base.index * 3 + n + 1)
                    for s in range(tile.f_blocks):
                        u = tile.units_before(n, True) + s
                        shape = dict(i=QCHUNKS, j=tile.side)
                        add(base.units + u, u,
                            summed[u % 2][:, 0:QCHUNKS * P].rearrange("p (i j b) -> p i j b", **shape),
                            turned[u % 2][:, 0:QCHUNKS * P].rearrange("p (i j b) -> p i j b", **shape),
                            units3(feat[:, 0:FC - 1, 0:m], tile, QCHUNKS, tile.f_blocks, s))
                    u = tile.units_before(n, True) + tile.f_blocks
                    add(base.units + u, u, summed[u % 2][:, 0:m], turned[u % 2][:, 0:m], feat[:, FC - 1, 0:m])
                    for _ in range(pooled_after[n]):
                        add_halves(base.groups + group, group % 2)
                        group += 1

            dve.wait_ge(small_in, 48)
            for group in range(TILES[0] // GB):
                add_halves(group, group % 2)
            over_tiles(dve, body)

        @block.scalar
        def _(act):
            for name in kept:
                kind, n = name
                source = (w1_d if kind == "w1" else w2_d)[n]
                act.dma_start(kept[name][:, :, :], source.rearrange("(k p) n -> p k n", p=P)).then_inc(kept_in[name], 16)

            def copy_group(group, place):
                act.wait_ge(group_turned, group + 1)
                nc.scalar.activation(pooled[:, :, place * GB:(place + 1) * GB],
                                     pool_ps[:, 0:FC * GB].rearrange("p (k b) -> p k b", k=FC),
                                     ACT.Copy).then_inc(group_pooled, 1)

            def copy_bank(bank_index, s, width):
                act.wait_ge(bank_done, bank_index + 1)
                nc.scalar.activation(by_batch[:, s * width:(s + 1) * width], acc[s][:, 0:width],
                                     ACT.Copy).then_inc(bank_copied, 1)

            def rectify(unit, out, source):
                act.wait_ge(unit_added, unit + 1)
                nc.scalar.activation(out, source, ACT.Relu).then_inc(unit_ready, 1)

            def body(base, pooled_after, last):
                tile, m = base.tile, base.tile.m
                group = 0
                for n in range(3):
                    blocks, width = tile.h_blocks(n), tile.h_width(n)
                    for s in range(blocks):
                        copy_bank(base.banks + tile.banks_before(n, False) + s, s, width)
                    for s in range(blocks):
                        u = tile.units_before(n, False) + s
                        rectify(base.units + u, units3(hidden[:, 0:HC[n], 0:m], tile, width // P, blocks, s),
                                summed[u % 2][:, 0:width].rearrange("p (i j b) -> p i j b", j=tile.side, b=m))
                    for s in range(tile.f_blocks):
                        copy_bank(base.banks + tile.banks_before(n, True) + s, s, QUAD)
                    for s in range(tile.f_blocks):
                        u = tile.units_before(n, True) + s
                        rectify(base.units + u,
                                units3(feat[:, 0:FC - 1, 0:m], tile, QCHUNKS, tile.f_blocks, s),
                                summed[u % 2][:, 0:QCHUNKS * P].rearrange("p (i j b) -> p i j b", j=tile.side, b=m))
                    u = tile.units_before(n, True) + tile.f_blocks
                    rectify(base.units + u, feat[:, FC - 1, 0:m], summed[u % 2][:, 0:m])
                    if n == 2:
                        act.wait_ge(lin_done, base.index + 1)
                        nc.scalar.activation(y[0:1, bass.ds(base.batches, m)], lin_ps[0:1, 0:m], ACT.Sigmoid,
                                             bias=lin_b[0:1, 0:1]).then_inc(y_ready, 1)
                    for _ in range(pooled_after[n]):
                        copy_group(base.groups + group, group)
                        group += 1

            for group in range(TILES[0] // GB):
                copy_group(group, group)
            over_tiles(act, body)

        @block.tensor
        def _(pe):
            def pool_group(group, buf, wait=True):
                pe.wait_ge(halves_added, group + 1)
                if wait:
                    pe.wait_ge(group_pooled, group)
                for k in range(FC):
                    last = nc.tensor.matmul(pool_ps[:, k * GB:(k + 1) * GB], rows[buf][:, 0, k * P:(k + 1) * P], sel,
                                            start=True, stop=True)
                last.then_inc(group_turned, 1)

            def product(base, matrix, order, source, first_unit, width, blocks, slab):
                tile, m = base.tile, base.tile.m
                seen = -1
                for at, (k, unit) in enumerate(order):
                    if first_unit is not None and unit > seen:
                        pe.wait_ge(unit_ready, base.units + first_unit + unit + 1)
                        seen = unit
                    if slab is None:
                        weights = kept[matrix][:, k, :]
                    else:
                        i = slab + at
                        pe.wait_ge(slot_in[i % SLOTS], base.index * (16 * slot_loads(i % SLOTS)) + 16 * (i // SLOTS + 1))
                        weights = slots[i % SLOTS]
                    for s in range(blocks):
                        for j in range(tile.side):
                            column = (j * blocks + s) * width
                            last = nc.tensor.matmul(acc[s][j * m:(j + 1) * m, 0:width], source[:, k, 0:m],
                                                    weights[:, column:column + width],
                                                    start=at == 0, stop=at == len(order) - 1)
                        if at == len(order) - 1:
                            last.then_inc(bank_done, 1)
                    if slab is not None and at < len(order) - 1:
                        last.then_inc(slabs_used, 1)

            def turn(base, u, bank_index, s, width, per, after_slab):
                pe.wait_ge(bank_copied, bank_index + 1)
                if u >= 2:
                    pe.wait_ge(unit_added, base.units + u - 1)
                for i in range(per):
                    last = nc.tensor.transpose(turned[u % 2][:, i * P:(i + 1) * P],
                                               by_batch[:, s * width + i * P:s * width + (i + 1) * P], ident)
                    if i == 0 and after_slab:
                        last.then_inc(slabs_used, 1)
                last.then_inc(unit_turned, 1)

            def body(base, pooled_after, last_tile):
                tile, m = base.tile, base.tile.m
                pe.wait_ge(group_pooled, base.groups)
                group = 0
                for n in range(3):
                    width, blocks = tile.h_width(n), tile.h_blocks(n)
                    if n == 0:
                        product(base, ("w1", 0), [(k, 0) for k in range(FC)], pooled, None, width, blocks, 0)
                    else:
                        product(base, ("w1", n), tile.f_order(), feat, tile.units_before(n - 1, True), width, blocks,
                                FC + HC[0] if n == 1 else None)
                    for s in range(blocks):
                        u = tile.units_before(n, False) + s
                        turn(base, u, base.banks + tile.banks_before(n, False) + s, s, width, width // P,
                             n < 2 and s == 0)
                    product(base, ("w2", n), tile.h_order(n), hidden, tile.units_before(n, False), QUAD,
                            tile.f_blocks, FC if n == 0 else None)
                    for s in range(tile.f_blocks):
                        u = tile.units_before(n, True) + s
                        turn(base, u, base.banks + tile.banks_before(n, True) + s, s, QUAD, QCHUNKS,
                             n == 0 and s == 0)
                    u = tile.units_before(n, True) + tile.f_blocks
                    pe.wait_ge(unit_added, base.units + u - 1)
                    for j in range(tile.side):
                        for s in range(tile.f_blocks):
                            q = j * tile.f_blocks + s
                            rest = s * QUAD + QCHUNKS * P
                            last = nc.tensor.matmul(turned[u % 2][q * REST:(q + 1) * REST, 0:m],
                                                    by_batch[:, rest:rest + REST],
                                                    ident[:, j * m:(j + 1) * m], start=True, stop=True)
                    last.then_inc(unit_turned, 1)
                    if n == 2:
                        pe.wait_ge(unit_ready, base.units + tile.units_before(3, False))
                        for k in range(FC):
                            last = nc.tensor.matmul(lin_ps[0:1, 0:m], params[:, LIN_W + k:LIN_W + k + 1],
                                                    feat[:, k, 0:m], start=k == 0, stop=k == FC - 1)
                        last.then_inc(lin_done, 1)
                    for _ in range(pooled_after[n]):
                        pool_group(base.groups + group, group % 2)
                        group += 1

            pe.wait_ge(small_in, 48)
            for group in range(TILES[0] // GB):
                pool_group(group, group % 2, group > 0)
            for matrix in kept_in:
                pe.wait_ge(kept_in[matrix], 16)
            over_tiles(pe, body)


def kernel(**inputs):
    import numpy as np
    import concourse.bacc as bacc
    from concourse.bass_utils import run_bass_kernel_spmd

    def given(name):
        return np.ascontiguousarray(inputs["L0_rec_" + name])

    x = np.asarray(inputs["r_x"])
    idx = x.reshape(GROUPS, GB, FIELDS, HALVES, QUARTERS).transpose(4, 1, 0, 2, 3)
    idx = np.ascontiguousarray(idx.reshape(P, GROUPS * GATHERS))

    consts = np.zeros((P, CONSTS), np.float32)
    consts[:, IDENT:IDENT + P] = np.eye(P)
    consts[:, SEL:SEL + GB] = np.tile(np.eye(GB), (QUARTERS, 1))

    def on_partitions(a):
        return a.reshape(-1, P).T

    params = np.ascontiguousarray(np.concatenate(
        [on_partitions(given(f"b1_{n}")) for n in range(3)] + [on_partitions(given(f"b2_{n}")) for n in range(3)]
        + [on_partitions(given("lin_w"))], axis=1))

    def quads(w):
        rows = w.shape[0]
        whole = w[:, :QUADS * QCHUNKS * P].reshape(rows, QUADS, QCHUNKS * P)
        rest = w[:, QUADS * QCHUNKS * P:].reshape(rows, QUADS, REST)
        return np.ascontiguousarray(np.concatenate([whole, rest], axis=2).reshape(rows, IN_DIM))

    arrays = {"idx": idx, "table": given("emb_table"), "consts_in": consts, "params_in": params,
              "lin_b_in": given("lin_b").reshape(1, 1)}
    for n in range(3):
        arrays[f"w1_{n}"] = given(f"w1_{n}")
        arrays[f"w2_{n}"] = quads(given(f"w2_{n}"))

    nc = bacc.Bacc("TRN2", target_bir_lowering=False, num_devices=1)
    d = {name: nc.dram_tensor(name, a.shape, mybir.dt.from_np(a.dtype), kind="ExternalInput").ap()
         for name, a in arrays.items()}
    out = nc.dram_tensor("out", (1, BATCH), F32, kind="ExternalOutput").ap()
    recommender(nc, d["idx"], d["table"], d["consts_in"], d["params_in"], d["lin_b_in"],
                [d[f"w1_{n}"] for n in range(3)], [d[f"w2_{n}"] for n in range(3)], out)
    r = run_bass_kernel_spmd(nc, [arrays], core_ids=[0])
    return r.results[0]["out"].reshape(BATCH, 1)
```

```python
from contextlib import ExitStack

import concourse.bass as bass
from concourse import mybir

F32 = mybir.dt.float32
I32 = mybir.dt.int32
ALU = mybir.AluOpType
ACT = mybir.ActivationFunctionType
AX = mybir.AxisListType

P = 128
BATCH, FIELDS, LOOKUPS, DIM = 512, 26, 8, 64
IN_DIM = FIELDS * DIM
HIDDENS = (1024, 1024, 512)
FC = IN_DIM // P
FPC = P // DIM
HC = [h // P for h in HIDDENS]

QUADS = 4
QCHUNKS = FC // QUADS
REST = P // QUADS
QUAD = QCHUNKS * P + REST

LOOP_TILES = 2
TILES = [128, 128, 128, 64, 64]
FULL = TILES.count(P)
REDUCED_AFTER = [[1, 1, 1, 1, 1, 1], [1, 1, 1, 1, 1, 1], [2, 2, 3, 2, 1, 1], [1, 1, 1, 1, 1, 1], [0] * 6]
BAG_UNITS = [[4, 4, 4, 1]] * FULL + [[7, 6], [4, 3, 2, 2, 1, 1]]

DMAS = FPC * LOOKUPS
ROUNDS = FULL + 1
ROW_BUFS = 5
PAIRS = [(k, min(k + 2, FC)) for k in range(0, FC, 2)]
AHEAD = 2

SLABS = FC + HC[0] + FC
SLOTS = 7
BANKWISE = 4

IDENT, HALVES, CONSTS = 0, P, P + P // 2
B1 = [0, HC[0], HC[0] + HC[1]]
B2 = [sum(HC) + FC * n for n in range(3)]
LIN_W = sum(HC) + 3 * FC
PARAMS = LIN_W + FC


class Tile:

    def __init__(self, i):
        self.m = TILES[i]
        self.side = P // self.m
        self.f_blocks = QUADS // self.side
        self.f_units = self.f_blocks + 1
        self.bag_units = BAG_UNITS[i]
        self.reduced_after = REDUCED_AFTER[i]
        self.last = i == len(TILES) - 1

    def h_width(self, n):
        return min(512, HIDDENS[n] // self.side // 2)

    def h_blocks(self, n):
        return HIDDENS[n] // self.side // self.h_width(n)

    def h_order(self, n):
        per, blocks = self.h_width(n) // P, self.h_blocks(n)
        return [((j * blocks + s) * per + i, s) for s in range(blocks) for j in range(self.side) for i in range(per)]

    def f_order(self):
        out = [(QCHUNKS * (j * self.f_blocks + s) + i, s)
               for s in range(self.f_blocks) for j in range(self.side) for i in range(QCHUNKS)]
        return out + [(FC - 1, self.f_blocks)]

    def bag_order(self):
        return [(k, u) for u, n in enumerate(self.bag_units) for k in range(sum(self.bag_units[:u]), sum(self.bag_units[:u]) + n)]

    def units_before(self, n, features=False):
        return sum(self.h_blocks(i) + self.f_units for i in range(n)) + (self.h_blocks(n) if features else 0)

    def banks_before(self, n, features=False):
        return sum(self.h_blocks(i) + self.f_blocks for i in range(n)) + (self.h_blocks(n) if features else 0)

    def slabs(self):
        return ([(("w1", 0), k) for k in range(FC)] + [(("w2", 0), k) for k, _ in self.h_order(0)]
                + [(("w1", 1), k) for k, _ in self.f_order()])


def slot_loads(slot):
    return len(range(slot, SLABS, SLOTS))


def buf_units(buf):
    return len(range(buf, FC, ROW_BUFS))


class Base:

    def __init__(self, index, tile_number):
        self.index = index
        self.tile = Tile(tile_number)
        if tile_number < FULL:
            first = Tile(0)
            self.units = index * first.units_before(3)
            self.banks = index * first.banks_before(3)
            self.batches = index * first.m
            self.bag_units = index * len(first.bag_units)
        else:
            before = [Tile(i) for i in range(tile_number)]
            self.units = sum(x.units_before(3) for x in before)
            self.banks = sum(x.banks_before(3) for x in before)
            self.batches = sum(x.m for x in before)
            self.bag_units = sum(len(x.bag_units) for x in before)


def over_tiles(eng, body):
    with eng.Fori(0, LOOP_TILES) as t:
        body(Base(t, 0))
    for t in range(LOOP_TILES, len(TILES)):
        body(Base(t, t))


def of_block(ap, tile, per, blocks, s):
    return ap.rearrange("p (j s i) b -> p s i j b", j=tile.side, s=blocks, i=per)[:, s]


def by_side(ap, tile, per):
    return ap[:, 0:per * P].rearrange("p (i j b) -> p i j b", i=per, j=tile.side)


def recommender(nc, idx_d, table_d, consts_d, params_d, lin_b_d, w1_d, w2_d, out_d):
    with ExitStack() as ctx:
        def sb(name, shape, dt=F32):
            return ctx.enter_context(nc.sbuf_tensor(name, shape, dt))

        def sem(name):
            return ctx.enter_context(nc.semaphore(name))

        idx_all = sb("idx_all", [P, ROUNDS * FC * DMAS], I32)
        idx_now = sb("idx_now", [P, FC * DMAS], I32)
        rows = [sb(f"rows{i}", [P, DMAS * DIM]) for i in range(ROW_BUFS)]
        bags = sb("bags", [P, FC, P])
        feat = sb("feat", [P, FC, P])
        hidden = sb("hidden", [P, max(HC), P])
        by_batch = sb("by_batch", [P, QUADS * QUAD])
        summed = [sb(f"summed{i}", [P, 512]) for i in range(2)]
        consts = sb("consts", [P, CONSTS])
        params = sb("params", [P, PARAMS])
        lin_b = sb("lin_b", [1, 1])
        y = sb("y", [1, BATCH])
        slots = [sb(f"slot{i}", [P, IN_DIM]) for i in range(SLOTS)]
        kept = {("w2", 1): sb("kept_w2_1", [P, HC[1], IN_DIM]),
                ("w1", 2): sb("kept_w1_2", [P, FC, HIDDENS[2]]),
                ("w2", 2): sb("kept_w2_2", [P, HC[2], IN_DIM])}
        ident = consts[:, IDENT:IDENT + P]
        halves = consts[:, HALVES:HALVES + P // 2]

        def bank(name):
            return ctx.enter_context(nc.psum_tensor(name, [P, 512], F32))

        acc = [bank(f"acc{i}") for i in range(QUADS)]
        turned = [bank(f"turned{i}") for i in range(2)]
        lin_ps = bank("lin_ps")

        idx_in = sem("idx_in")
        small_in = sem("small_in")
        kept_in = {("w2", 1): sem("kept_w2_1_in"), ("w1", 2): sem("kept_w1_2_in"), ("w2", 2): sem("kept_w2_2_in")}
        slot_in = [sem(f"slot_in{i}") for i in range(SLOTS)]
        slabs_used = sem("slabs_used")
        idx_copied = sem("idx_copied")
        rows_in = [sem(f"rows_in{i}") for i in range(ROW_BUFS)]
        rows_added = sem("rows_added")
        bags_ready = sem("bags_ready")
        bags_turned = sem("bags_turned")
        bags_copied = sem("bags_copied")
        bank_done = sem("bank_done")
        bank_copied = sem("bank_copied")
        unit_turned = sem("unit_turned")
        unit_added = sem("unit_added")
        unit_ready = sem("unit_ready")
        residual_ready = sem("residual_ready")
        lin_done = sem("lin_done")
        y_ready = sem("y_ready")
        stored = sem("stored")

        block = ctx.enter_context(nc.Block())

        @block.sync
        def _(sp):
            sp.dma_start(idx_all[:, :], idx_d).then_inc(idx_in, 16)
            sp.dma_start(consts[:, :], consts_d).then_inc(small_in, 16)
            sp.dma_start(params[:, :], params_d).then_inc(small_in, 16)
            sp.dma_start(lin_b[:, :], lin_b_d).then_inc(small_in, 16)

            def load(tile, i):
                (kind, n), k = tile.slabs()[i]
                source = (w1_d if kind == "w1" else w2_d)[n][k * P:(k + 1) * P, :]
                sp.dma_start(slots[i % SLOTS][:, 0:source.shape[1]], source).then_inc(slot_in[i % SLOTS], 16)

            for i in range(SLOTS):
                load(Tile(0), i)

            def body(base):
                for i in range(SLOTS, SLABS):
                    sp.wait_ge(slabs_used, base.index * SLABS + i - SLOTS + 1)
                    load(base.tile, i)
                if not base.tile.last:
                    for i in range(SLOTS):
                        sp.wait_ge(slabs_used, base.index * SLABS + max(range(i, SLABS, SLOTS)) + 1)
                        load(base.tile, i)

            over_tiles(sp, body)
            sp.wait_ge(y_ready, len(TILES))
            sp.dma_start(out_d, y[:, :]).then_inc(stored, 16)
            sp.wait_ge(stored, 16)

        @block.gpsimd
        def _(pool):
            def copy_indices(round_, pair):
                begin, end = (k * DMAS for k in PAIRS[pair])
                nc.gpsimd.tensor_copy(idx_now[:, begin:end],
                                      idx_all[:, bass.ds(round_ * (FC * DMAS) + begin, end - begin)],
                                      ).then_inc(idx_copied, 1)

            def gather(round_, pair, units_added, last=False):
                begin, end = PAIRS[pair]
                pool.wait_ge(idx_copied, round_ * len(PAIRS) + pair + 1)
                if units_added is not None:
                    pool.wait_ge(rows_added, units_added)
                if not last:
                    if pair + 1 < len(PAIRS):
                        copy_indices(round_, pair + 1)
                    else:
                        copy_indices(round_ + 1, 0)
                for k in range(begin, end):
                    for g in range(DMAS):
                        nc.gpsimd.indirect_dma_start(
                            rows[k % ROW_BUFS][:, g * DIM:(g + 1) * DIM], None, table_d,
                            bass.IndirectOffsetOnAxis(ap=idx_now[:, k * DMAS + g:k * DMAS + g + 1], axis=0),
                        ).then_inc(rows_in[k % ROW_BUFS], 16)

            def rest_of_round(round_, last=False):
                for pair in range(AHEAD, len(PAIRS)):
                    gather(round_, pair, round_ * FC + PAIRS[pair][1] - ROW_BUFS, last and pair == len(PAIRS) - 1)

            pool.wait_ge(idx_in, 16)
            copy_indices(0, 0)
            for pair in range(AHEAD):
                gather(0, pair, None)
            with pool.Fori(0, ROUNDS - 1) as round_:
                rest_of_round(round_)
                for pair in range(AHEAD):
                    held = max(u for k in range(*PAIRS[pair]) for u in range(k, FC, ROW_BUFS))
                    gather(round_ + 1, pair, round_ * FC + held + 1)
            rest_of_round(ROUNDS - 1, last=True)

        @block.vector
        def _(dve):
            def add_rows(index, k, tile):
                if tile.side == 1:
                    round_, unit, part, parts = index, k, 0, 1
                else:
                    round_, (unit, part), parts = FULL, divmod((index - FULL) * FC + k, 2), 2
                buf, size = unit % ROW_BUFS, DMAS * DIM // parts
                dve.wait_ge(rows_in[buf], round_ * (16 * DMAS * buf_units(buf)) + 16 * DMAS * (unit // ROW_BUFS + 1))
                reduce = nc.vector.tensor_reduce(
                    bags[:, k, :].rearrange("p (f d) -> p f d", f=FPC),
                    rows[buf][:, part * size:(part + 1) * size].rearrange("p (f l d) -> p f d l", f=FPC, d=DIM),
                    AX.X, ALU.add).then_inc(bags_ready, 1)
                if part == parts - 1:
                    dve.wait_ge(bags_ready, index * FC + k + 1)
                    dve.sem_inc(rows_added, 1)

            def add(unit, u, out, turned_ap, other):
                dve.wait_ge(unit_turned, unit + 1)
                if u >= 2:
                    dve.wait_ge(unit_ready, unit - 1)
                nc.vector.tensor_tensor(out, turned_ap, other, ALU.add).then_inc(unit_added, 1)

            def body(base):
                tile, m = base.tile, base.tile.m
                after = Tile(base.index + 1) if isinstance(base.index, int) and not tile.last else Tile(0)
                for k in range(early(base), FC):
                    add_rows(base.index, k, tile)
                done = 0
                for n in range(3):
                    blocks, per = tile.h_blocks(n), tile.h_width(n) // P
                    bias = params[:, B1[n]:B1[n] + HC[n]].unsqueeze(2).to_broadcast([P, HC[n], m])
                    for s in range(blocks):
                        u = tile.units_before(n) + s
                        add(base.units + u, u, by_side(summed[u % 2], tile, per), by_side(turned[u % 2], tile, per),
                            of_block(bias, tile, per, blocks, s))
                    dve.wait_ge(bank_done, base.banks + tile.banks_before(n, True))
                    nc.vector.tensor_tensor(feat[:, :, 0:m], feat[:, :, 0:m],
                                            params[:, B2[n]:B2[n] + FC].unsqueeze(2).to_broadcast([P, FC, m]),
                                            ALU.add).then_inc(residual_ready, 1)
                    for _ in range(tile.reduced_after[2 * n]):
                        add_rows(base.index + 1, done, after)
                        done += 1
                    dve.wait_ge(residual_ready, base.index * 3 + n + 1)
                    for s in range(tile.f_blocks):
                        u = tile.units_before(n, True) + s
                        add(base.units + u, u, by_side(summed[u % 2], tile, QCHUNKS),
                            by_side(turned[u % 2], tile, QCHUNKS),
                            of_block(feat[:, 0:FC - 1, 0:m], tile, QCHUNKS, tile.f_blocks, s))
                    u = tile.units_before(n, True) + tile.f_blocks
                    add(base.units + u, u, summed[u % 2][:, 0:m], turned[u % 2][:, 0:m], feat[:, FC - 1, 0:m])
                    for _ in range(tile.reduced_after[2 * n + 1]):
                        add_rows(base.index + 1, done, after)
                        done += 1

            def early(base):
                if not isinstance(base.index, int):
                    return sum(REDUCED_AFTER[0])
                return sum(REDUCED_AFTER[base.index - 1])

            dve.wait_ge(small_in, 48)
            for k in range(sum(REDUCED_AFTER[0])):
                add_rows(0, k, Tile(0))
            over_tiles(dve, body)

        @block.scalar
        def _(act):
            for matrix in kept:
                kind, n = matrix
                source = (w1_d if kind == "w1" else w2_d)[n]
                act.dma_start(kept[matrix][:, :, :], source.rearrange("(k p) n -> p k n", p=P)).then_inc(kept_in[matrix], 16)

            def copy_bags(base, u):
                tile, m = base.tile, base.tile.m
                begin = sum(tile.bag_units[:u])
                count = tile.bag_units[u]
                act.wait_ge(bags_turned, base.bag_units + u + 1)
                nc.scalar.activation(feat[:, begin:begin + count, 0:m],
                                     turned[u % 2][:, 0:count * m].rearrange("p (k b) -> p k b", k=count),
                                     ACT.Copy).then_inc(bags_copied, 1)

            def copy_bank(bank_index, s, width):
                act.wait_ge(bank_done, bank_index + 1)
                nc.scalar.activation(by_batch[:, s * width:(s + 1) * width], acc[s][:, 0:width],
                                     ACT.Copy).then_inc(bank_copied, 1)

            def rectify(unit, out, source):
                act.wait_ge(unit_added, unit + 1)
                nc.scalar.activation(out, source, ACT.Relu).then_inc(unit_ready, 1)

            def layer(base, first_bank, first_unit, blocks, per, width, target):
                tile = base.tile
                for s in range(blocks + 1):
                    if s < blocks:
                        copy_bank(base.banks + first_bank + s, s, width)
                    if s:
                        u = first_unit + s - 1
                        rectify(base.units + u, of_block(target, tile, per, blocks, s - 1),
                                by_side(summed[u % 2], tile, per))

            def body(base):
                tile, m = base.tile, base.tile.m
                for u in range(len(tile.bag_units)):
                    copy_bags(base, u)
                for n in range(3):
                    layer(base, tile.banks_before(n), tile.units_before(n), tile.h_blocks(n), tile.h_width(n) // P,
                          tile.h_width(n), hidden[:, 0:HC[n], 0:m])
                    layer(base, tile.banks_before(n, True), tile.units_before(n, True), tile.f_blocks, QCHUNKS, QUAD,
                          feat[:, 0:FC - 1, 0:m])
                    u = tile.units_before(n, True) + tile.f_blocks
                    rectify(base.units + u, feat[:, FC - 1, 0:m], summed[u % 2][:, 0:m])
                act.wait_ge(lin_done, base.index + 1)
                nc.scalar.activation(y[0:1, bass.ds(base.batches, m)], lin_ps[0:1, 0:m], ACT.Sigmoid,
                                     bias=lin_b[0:1, 0:1]).then_inc(y_ready, 1)

            over_tiles(act, body)

        @block.tensor
        def _(pe):
            def turn_bags(base, u):
                tile, m = base.tile, base.tile.m
                begin = sum(tile.bag_units[:u])
                count = tile.bag_units[u]
                pe.wait_ge(bags_ready, base.index * FC + begin + count)
                if u >= 2:
                    pe.wait_ge(bags_copied, base.bag_units + u - 1)
                for i in range(count):
                    out, bag = turned[u % 2][:, i * m:(i + 1) * m], bags[:, begin + i, :]
                    if tile.side == 1:
                        last = nc.tensor.transpose(out, bag, ident)
                    else:
                        last = nc.tensor.matmul(out, bag, halves, start=True, stop=True)
                last.then_inc(bags_turned, 1)

            def turn(base, u, bank_index, s, width, per, after_slab=False):
                pe.wait_ge(bank_copied, bank_index + 1)
                if u >= 2:
                    pe.wait_ge(unit_added, base.units + u - 1)
                for i in range(per):
                    last = nc.tensor.transpose(turned[u % 2][:, i * P:(i + 1) * P],
                                               by_batch[:, s * width + i * P:s * width + (i + 1) * P], ident)
                    if i == 0 and after_slab:
                        last.then_inc(slabs_used, 1)
                last.then_inc(unit_turned, 1)

            def turn_rest(base, n):
                tile, m = base.tile, base.tile.m
                u = tile.units_before(n, True) + tile.f_blocks
                pe.wait_ge(unit_added, base.units + u - 1)
                for j in range(tile.side):
                    for s in range(tile.f_blocks):
                        q, rest = j * tile.f_blocks + s, s * QUAD + QCHUNKS * P
                        last = nc.tensor.matmul(turned[u % 2][q * REST:(q + 1) * REST, 0:m],
                                                by_batch[:, rest:rest + REST], ident[:, j * m:(j + 1) * m],
                                                start=True, stop=True)
                last.then_inc(unit_turned, 1)

            def product(base, matrix, order, source, before_unit, width, blocks, first_bank, first_unit, slab,
                        bankwise=BANKWISE):
                tile, m = base.tile, base.tile.m

                def weights_at(at):
                    if slab is None:
                        return kept[matrix][:, order[at][0], :]
                    return slots[(slab + at) % SLOTS]

                def arrive(at):
                    before_unit(order[at][1], at == 0 or order[at][1] != order[at - 1][1])
                    if slab is not None:
                        slot = (slab + at) % SLOTS
                        pe.wait_ge(slot_in[slot], base.index * (16 * slot_loads(slot)) + 16 * ((slab + at) // SLOTS + 1))

                def step(at, s):
                    for j in range(tile.side):
                        column = (j * blocks + s) * width
                        last = nc.tensor.matmul(acc[s][j * m:(j + 1) * m, 0:width], source[:, order[at][0], 0:m],
                                                weights_at(at)[:, column:column + width],
                                                start=at == 0, stop=at == len(order) - 1)
                    return last

                whole = len(order) - bankwise
                for at in range(whole):
                    arrive(at)
                    for s in range(blocks):
                        last = step(at, s)
                    if slab is not None:
                        last.then_inc(slabs_used, 1)
                for s in range(blocks):
                    for at in range(whole, len(order)):
                        if s == 0:
                            arrive(at)
                        last = step(at, s)
                        if at == len(order) - 1:
                            last.then_inc(bank_done, 1)
                        elif slab is not None and s == blocks - 1:
                            last.then_inc(slabs_used, 1)
                        if s and at - whole == (bankwise - 1) // 2:
                            turn(base, first_unit + s - 1, base.banks + first_bank + s - 1, s - 1, width, width // P)
                turn(base, first_unit + blocks - 1, base.banks + first_bank + blocks - 1, blocks - 1, width,
                     width // P, after_slab=slab is not None)

            def body(base):
                tile, m = base.tile, base.tile.m

                def bags_first(u, new):
                    if new:
                        if tile.last or u == 0:
                            turn_bags(base, u)
                        if not tile.last and u + 1 < len(tile.bag_units):
                            turn_bags(base, u + 1)
                        pe.wait_ge(bags_copied, base.bag_units + u + 1)

                def hidden_first(n):
                    def before_unit(u, new):
                        if new:
                            pe.wait_ge(unit_ready, base.units + tile.units_before(n) + u + 1)
                    return before_unit

                def features_first(n):
                    def before_unit(u, new):
                        if new and u == 1:
                            turn_rest(base, n)
                        if new:
                            pe.wait_ge(unit_ready, base.units + tile.units_before(n, True) + u + 1)
                    return before_unit

                for n in range(3):
                    product(base, ("w1", n), tile.f_order() if n else tile.bag_order(), feat,
                            features_first(n - 1) if n else bags_first, tile.h_width(n), tile.h_blocks(n),
                            tile.banks_before(n), tile.units_before(n), (0, FC + HC[0], None)[n],
                            1 if tile.last and not n else BANKWISE)
                    product(base, ("w2", n), tile.h_order(n), hidden, hidden_first(n), QUAD, tile.f_blocks,
                            tile.banks_before(n, True), tile.units_before(n, True), FC if n == 0 else None)
                before_unit, seen = features_first(2), None
                for at, (k, unit) in enumerate(tile.f_order()):
                    before_unit(unit, unit != seen)
                    seen = unit
                    last = nc.tensor.matmul(lin_ps[0:1, 0:m], params[:, LIN_W + k:LIN_W + k + 1], feat[:, k, 0:m],
                                            start=at == 0, stop=at == FC - 1)
                last.then_inc(lin_done, 1)

            pe.wait_ge(small_in, 48)
            for matrix in kept_in:
                pe.wait_ge(kept_in[matrix], 16)
            over_tiles(pe, body)


def kernel(**inputs):
    import numpy as np
    import concourse.bacc as bacc
    from concourse.bass_utils import run_bass_kernel_spmd

    def given(name):
        return np.ascontiguousarray(inputs["L0_rec_" + name])

    x = np.asarray(inputs["r_x"])
    full, half = x[:FULL * P], x[FULL * P:]
    full = full.reshape(FULL, P, FIELDS * LOOKUPS).transpose(1, 0, 2).reshape(P, -1)
    half = half.reshape(-1, P // 2, FIELDS, 2, LOOKUPS // 2).transpose(3, 1, 0, 2, 4).reshape(P, -1)
    idx = np.ascontiguousarray(np.concatenate([full, half], axis=1))

    consts = np.zeros((P, CONSTS), np.float32)
    consts[:, IDENT:IDENT + P] = np.eye(P)
    consts[:, HALVES:HALVES + P // 2] = np.tile(np.eye(P // 2), (2, 1))

    def on_partitions(a):
        return a.reshape(-1, P).T

    params = np.ascontiguousarray(np.concatenate(
        [on_partitions(given(f"b1_{n}")) for n in range(3)] + [on_partitions(given(f"b2_{n}")) for n in range(3)]
        + [on_partitions(given("lin_w"))], axis=1))

    def quads(w):
        rows = w.shape[0]
        whole = w[:, :QUADS * QCHUNKS * P].reshape(rows, QUADS, QCHUNKS * P)
        rest = w[:, QUADS * QCHUNKS * P:].reshape(rows, QUADS, REST)
        return np.ascontiguousarray(np.concatenate([whole, rest], axis=2).reshape(rows, IN_DIM))

    arrays = {"idx": idx, "table": given("emb_table"), "consts_in": consts, "params_in": params,
              "lin_b_in": given("lin_b").reshape(1, 1)}
    for n in range(3):
        arrays[f"w1_{n}"] = given(f"w1_{n}")
        arrays[f"w2_{n}"] = quads(given(f"w2_{n}"))

    nc = bacc.Bacc("TRN2", target_bir_lowering=False, num_devices=1)
    d = {name: nc.dram_tensor(name, a.shape, mybir.dt.from_np(a.dtype), kind="ExternalInput").ap()
         for name, a in arrays.items()}
    out = nc.dram_tensor("out", (1, BATCH), F32, kind="ExternalOutput").ap()
    recommender(nc, d["idx"], d["table"], d["consts_in"], d["params_in"], d["lin_b_in"],
                [d[f"w1_{n}"] for n in range(3)], [d[f"w2_{n}"] for n in range(3)], out)
    r = run_bass_kernel_spmd(nc, [arrays], core_ids=[0])
    return r.results[0]["out"].reshape(BATCH, 1)
```
